# Optimizing a Trainium2 kernel written in Bass

```python
import numpy as np
import jax
import jax.numpy as jnp

def _softmax(x, axis=-1):
    return jax.nn.softmax(x, axis=axis)

def _gelu(x):
    return jax.nn.gelu(x, approximate=True)

def _silu(x):
    return jax.nn.silu(x)

def _sigmoid(x):
    return jax.nn.sigmoid(x)

def _layernorm(x, axis=-1, eps=1e-05):
    m = jnp.mean(x, axis=axis, keepdims=True)
    v = jnp.var(x, axis=axis, keepdims=True)
    return (x - m) / jnp.sqrt(v + eps)

def _scatter_add(tgt, idx, src, axis=0):
    return tgt.at[idx].add(src)

def _segment_sum(src, seg, n):
    return jax.ops.segment_sum(src, seg, n)
kernel_name = 'mk_prb_d1_jaxref_r8_773d7e'

def setup_inputs(seed: int=0):
    np.random.seed(seed)
    _w = jnp.asarray

    def _L0_attn_setup():
        import jax, jax.numpy as jnp
        import numpy as np
        import math
        N_HEADS = 16
        DIM = 128
        B, S = (2, 256)

        def _split_heads(x, n_heads):
            b, s, d = x.shape
            dh = d // n_heads
            return x.reshape(b, s, n_heads, dh).transpose(0, 2, 1, 3)
        key = jax.random.key(seed)
        ks = jax.random.split(key, 9)
        std = 0.02
        inp = {'query': jax.random.normal(ks[0], (B, S, DIM), dtype=jnp.float32), 'mask': jnp.ones((B, S), dtype=jnp.int64), 'q_w': jax.random.normal(ks[1], (DIM, DIM), dtype=jnp.float32) * std, 'q_b': jnp.zeros((DIM,), dtype=jnp.float32), 'k_w': jax.random.normal(ks[2], (DIM, DIM), dtype=jnp.float32) * std, 'k_b': jnp.zeros((DIM,), dtype=jnp.float32), 'v_w': jax.random.normal(ks[3], (DIM, DIM), dtype=jnp.float32) * std, 'v_b': jnp.zeros((DIM,), dtype=jnp.float32), 'out_w': jax.random.normal(ks[4], (DIM, DIM), dtype=jnp.float32) * std, 'out_b': jnp.zeros((DIM,), dtype=jnp.float32)}
        return inp
    _L0_attn_in = _L0_attn_setup()

    def _L0_ffn_setup():
        import jax, jax.numpy as jnp
        import numpy as np
        B, S, D_MODEL, D_FF, E, R, TOP_K = (4, 256, 128, 512, 8, 16, 2)
        key = jax.random.key(seed)
        ks = jax.random.split(key, 9)
        sd = 1.0 / np.sqrt(D_MODEL)
        return {'hidden_states': jax.random.normal(ks[0], (B, S, D_MODEL), jnp.float32), 'wi': jax.random.normal(ks[1], (D_FF, D_MODEL), jnp.float32) * sd, 'bi': jax.random.normal(ks[2], (D_FF,), jnp.float32) * 0.01, 'wo': jax.random.normal(ks[3], (D_MODEL, D_FF), jnp.float32) * (1.0 / np.sqrt(D_FF)), 'bo': jax.random.normal(ks[4], (D_MODEL,), jnp.float32) * 0.01, 'lora_A': jax.random.normal(ks[5], (E, R, D_MODEL), jnp.float32) * sd, 'lora_B': jax.random.normal(ks[6], (E, D_FF, R), jnp.float32) * 0.02, 'gate_w': jax.random.normal(ks[7], (E, D_MODEL), jnp.float32) * sd, 'gate_b': jax.random.normal(ks[8], (E,), jnp.float32) * 0.01}
    _L0_ffn_in = _L0_ffn_setup()
    _d = {'L0_attn_query': _L0_attn_in['query'], 'L0_attn_mask': _L0_attn_in['mask'], 'L0_attn_q_w': _L0_attn_in['q_w'], 'L0_attn_q_b': _L0_attn_in['q_b'], 'L0_attn_k_w': _L0_attn_in['k_w'], 'L0_attn_k_b': _L0_attn_in['k_b'], 'L0_attn_v_w': _L0_attn_in['v_w'], 'L0_attn_v_b': _L0_attn_in['v_b'], 'L0_attn_out_w': _L0_attn_in['out_w'], 'L0_attn_out_b': _L0_attn_in['out_b'], 'L0_ffn_wi': _L0_ffn_in['wi'], 'L0_ffn_bi': _L0_ffn_in['bi'], 'L0_ffn_wo': _L0_ffn_in['wo'], 'L0_ffn_bo': _L0_ffn_in['bo'], 'L0_ffn_lora_A': _L0_ffn_in['lora_A'], 'L0_ffn_lora_B': _L0_ffn_in['lora_B'], 'L0_ffn_gate_w': _L0_ffn_in['gate_w'], 'L0_ffn_gate_b': _L0_ffn_in['gate_b']}
    _x0 = _d['L0_attn_query']
    _d['L0_attn_query'] = jax.random.normal(jax.random.fold_in(jax.random.key(seed), 1), (2, 2048, 128), dtype=_x0.dtype)
    del _x0
    return _d

def reference(L0_attn_query, L0_attn_mask, L0_attn_q_w, L0_attn_q_b, L0_attn_k_w, L0_attn_k_b, L0_attn_v_w, L0_attn_v_b, L0_attn_out_w, L0_attn_out_b, L0_ffn_wi, L0_ffn_bi, L0_ffn_wo, L0_ffn_bo, L0_ffn_lora_A, L0_ffn_lora_B, L0_ffn_gate_w, L0_ffn_gate_b):

    def _L0_attn_ref(query, mask, q_w, q_b, k_w, k_b, v_w, v_b, out_w, out_b):
        import jax, jax.numpy as jnp
        import numpy as np
        import math
        N_HEADS = 16
        DIM = 128
        B, S = (2, 256)

        def _split_heads(x, n_heads):
            b, s, d = x.shape
            dh = d // n_heads
            return x.reshape(b, s, n_heads, dh).transpose(0, 2, 1, 3)
        b, s, d = query.shape
        h = N_HEADS
        dh = d // h
        scale = math.sqrt(dh)
        q = _split_heads(query @ q_w.T + q_b, h) / scale
        k = _split_heads(query @ k_w.T + k_b, h)
        v = _split_heads(query @ v_w.T + v_b, h)
        scores = jnp.einsum('bhqd,bhkd->bhqk', q, k)
        attn = jax.nn.softmax(scores.astype(jnp.float32), axis=-1).astype(query.dtype)
        ctx = jnp.einsum('bhqk,bhkd->bhqd', attn, v)
        ctx = ctx.transpose(0, 2, 1, 3).reshape(b, s, d)
        out = ctx @ out_w.T + out_b
        return out

    def _L0_ffn_ref(hidden_states, wi, bi, wo, bo, lora_A, lora_B, gate_w, gate_b):
        import jax, jax.numpy as jnp
        import numpy as np
        B, S, D_MODEL, D_FF, E, R, TOP_K = (4, 256, 128, 512, 8, 16, 2)
        logits = jnp.einsum('bsd,ed->bse', hidden_states, gate_w) + gate_b
        scores = jax.nn.softmax(logits, axis=-1)
        top_v, top_i = jax.lax.top_k(scores, TOP_K)
        val_sum = top_v.sum(axis=-1)
        out = jnp.zeros_like(hidden_states)
        for e in range(E):
            count = (top_i == e).sum(axis=-1).astype(hidden_states.dtype)
            gate = count * val_sum
            inter = jnp.einsum('bsd,fd->bsf', hidden_states, wi) + bi + jnp.einsum('bsr,fr->bsf', jnp.einsum('bsd,rd->bsr', hidden_states, lora_A[e]), lora_B[e])
            h = jax.nn.relu(inter)
            expert_out = jnp.einsum('bsf,df->bsd', h, wo) + bo
            out = out + gate[..., None] * expert_out
        return out
    x = L0_attn_query
    xn = _layernorm(x, axis=-1)
    x = x + _L0_attn_ref(xn, L0_attn_mask, L0_attn_q_w, L0_attn_q_b, L0_attn_k_w, L0_attn_k_b, L0_attn_v_w, L0_attn_v_b, L0_attn_out_w, L0_attn_out_b) + _L0_ffn_ref(xn, L0_ffn_wi, L0_ffn_bi, L0_ffn_wo, L0_ffn_bo, L0_ffn_lora_A, L0_ffn_lora_B, L0_ffn_gate_w, L0_ffn_gate_b)
    return x

_drawn_inputs = setup_inputs


def setup_inputs(seed=0):
    import zlib

    import numpy as np

    out = dict(_drawn_inputs(seed))
    spreads = {'L0_attn_q_b': (0.0, 0.8),
     'L0_attn_k_b': (0.0, 0.8),
     'L0_attn_v_b': (0.0, 0.466),
     'L0_attn_out_b': (0.0, 0.1)}
    factors = {'L0_attn_q_w': 8.0,
     'L0_attn_k_w': 8.0,
     'L0_attn_v_w': 8.0,
     'L0_attn_out_w': 3.511,
     'L0_ffn_bi': 8.0,
     'L0_ffn_bo': 6.355,
     'L0_ffn_gate_b': 8.0}
    for name, (base, spread) in spreads.items():
        noise = np.random.default_rng([zlib.crc32(name.encode()), seed]).standard_normal(out[name].shape)
        drawn = base * np.exp(spread * noise) if base else spread * noise
        out[name] = jnp.asarray(drawn.astype(out[name].dtype))
    for name, factor in factors.items():
        out[name] = (out[name] * factor).astype(out[name].dtype)
    return out
```

```python
from contextlib import ExitStack

import concourse.bass as bass
from concourse import mybir

F32 = mybir.dt.float32
BF16 = mybir.dt.bfloat16
ALU = mybir.AluOpType
ACT = mybir.ActivationFunctionType
AX = mybir.AxisListType

P = 128
D = 128
H = 16
DH = D // H
B = 2
S = 2048
T = B * S
E, R = 8, 16
F = 512
FC = F // P
G = 512
GT = G // P
NG = T // G
EPS = 1e-5
SCALE = float(DH) ** -0.5

NPART = 3
Q_PART = (0, 0, 0, 1, 1, 2)
K_PART = (0, 1, 2, 0, 1, 0)
NSLOT = len(Q_PART)
DOTS = NSLOT * DH
HG = 4
NHG = H // HG
QC = S // G
NCH = B * NHG * QC
KT = S // P
KC = S // G
TILES = KT * HG
MAXOPS = 2 * KT
LEAD = 7
VW = DH + 1
W3 = D + E + E * R
LINKS = 21


class Chain:

    def __init__(self, engine, sem):
        self.engine, self.sem, self.base, self.n = engine, sem, 0, 0

    def link(self, ins):
        self.n += 1
        ins.then_inc(self.sem, 1)
        self.engine.wait_ge(self.sem, self.base + self.n)


def tokens_block(nc, io, keep):
    with ExitStack() as ctx:
        sb = lambda name, shape, dt=F32: ctx.enter_context(nc.sbuf_tensor(name, shape, dt))
        ps = lambda name, shape: ctx.enter_context(nc.psum_tensor(name, shape, F32))
        sem = lambda name: ctx.enter_context(nc.semaphore(name))

        x, ident, v_aug, y_tok = keep["x"], keep["ident"], keep["v_aug"], keep["y_tok"]
        wq, wk = sb("wq", [P, D]), sb("wk", [P, D])
        w3 = sb("w3", [P, W3])
        wi, lora_b, wo = sb("wi", [P, F]), sb("lora_b", [P, F]), sb("wo", [P, FC, D])
        qb, kb, qbs, bi = sb("qb", [P, 1]), sb("kb", [P, 1]), sb("qbs", [P, 1]), sb("bi", [P, FC])
        vb_row, gb_row, bo_row, ob_row = sb("vb_row", [P, D]), sb("gb_row", [P, E]), sb("bo_row", [P, D]), sb("ob_row", [P, D])
        bo2_row, rank_w = sb("bo2_row", [P, D]), sb("rank_w", [P, E])
        stats, mv, rstd = sb("stats", [P, GT, 6]), sb("mv", [P, GT, 2]), sb("rstd", [P, GT])
        var_eps, eps, minus_half = sb("var_eps", [P, GT]), sb("eps", [P, GT]), sb("minus_half", [P, GT])
        xn = sb("xn", [P, GT, D])
        xnT = [sb(f"xnT{i}", [P, G]) for i in range(2)]
        qk32, rest = sb("qk32", [P, 2, G]), sb("rest", [P, 2, G])
        parts = sb("parts", [P, 2, NPART, G], BF16)
        raw = sb("raw", [P, GT, W3])
        lg, ex, sc, sc2, eq = (sb(n, [P, GT, E]) for n in ("lg", "ex", "sc", "sc2", "eq"))
        mask = [sb(f"mask{s}", [P, GT, E]) for s in range(2)]
        mx, sm, m1, m2, wmax = (sb(n, [P, GT]) for n in ("mx", "sm", "m1", "m2", "wmax"))
        vs = [sb(f"vs{i}", [P, GT]) for i in range(2)]
        am = [sb(f"am{s}", [P, GT, E * R]) for s in range(2)]
        amT = [[sb(f"amT{i}{s}", [P, G]) for s in range(2)] for i in range(2)]
        xob = [sb(f"xob{i}", [P, GT, D]) for i in range(2)]
        hs = [[sb(f"hs{f}{s}", [P, G]) for s in range(2)] for f in range(2)]
        hT = sb("hT", [P, FC, G])
        y1, y2 = sb("y1", [P, GT, D]), sb("y2", [P, GT, D])

        psA = ps("psA", [P, G])
        psQK = ps("psQK", [P, 2, G])
        psV = ps("psV", [P, 2, G])
        psZ = ps("psZ", [P, 2, G])
        psY = ps("psY", [P, GT, D])

        x_first, x_rest, w_loaded, consts = sem("x_first"), sem("x_rest"), sem("w_loaded"), sem("consts")
        stats_ready, rstd_ready, xn_ready = sem("stats_ready"), sem("rstd_ready"), sem("xn_ready")
        xnT_turned, xnT_ready, qk_ps = sem("xnT_turned"), sem("xnT_ready"), sem("qk_ps")
        qk32_ready, hi_ready, rest_ready, mid_ready, parts_ready = (
            sem("qk32_ready"), sem("hi_ready"), sem("rest_ready"), sem("mid_ready"), sem("parts_ready"))
        parts_stored = sem("parts_stored")
        vga_ps, raw_copied, lg_ready, ex_ready, masks_ready = (
            sem("vga_ps"), sem("raw_copied"), sem("lg_ready"), sem("ex_ready"), sem("masks_ready"))
        v_kept, xob_ready, am_ready, amT_turned, amT_ready = (
            sem("v_kept"), sem("xob_ready"), sem("am_ready"), sem("amT_turned"), sem("amT_ready"))
        z_ready, z_read, h_added, y_ps, y_done = sem("z_ready"), sem("z_read"), sem("h_added"), sem("y_ps"), sem("y_done")
        dve_link, pool_link = sem("dve_link"), sem("pool_link")
        passed = sem("passed")
        NW = 15
        NCONST = 7 + E

        def hidden(part):
            if part > FC:
                return []
            pieces = [(part, 0)] * (part < FC) + [(part - 1, 1)] * (part > 0)
            return [(f, s, ORDER.index((f, s)) + 1) for f, s in pieces]

        ORDER = [(0, 0)] + [x for f in range(1, FC) for x in ((f, 0), (f - 1, 1))] + [(FC - 1, 1)]

        def schedule(project, experts, masked):
            def step(g, par, first=False, last=False):
                for part in range(FC):
                    if not first:
                        experts(part, g - 1, 1 - par)
                    project(part, g, par, first, last)
                if not first:
                    experts(FC, g - 1, 1 - par)
                masked(g, par, first, last)
                if not first:
                    experts(FC + 1, g - 1, 1 - par)
            return step

        def run(engine, step, experts, before_loop=None, per_pair=0, chain=None):
            step(0, 0, first=True)
            base = chain.n if chain else 0
            with engine.Fori(0, (NG - 2) // 2) as i:
                if chain:
                    chain.base, chain.n = i * per_pair + base, 0
                step(2 * i + 1, 1)
                step(2 * i + 2, 0)
            if chain:
                assert chain.n == per_pair, chain.n
                chain.base, chain.n = base + per_pair * ((NG - 2) // 2), 0
            step(NG - 1, 1, last=True)
            for part in range(FC + 2):
                experts(part, NG - 1, 1)

        block = ctx.enter_context(nc.Block())

        @block.sync
        def _(sp):
            sp.dma_start(x[:, 0:GT, :], io["x"][:, 0:GT, :]).then_inc(x_first, 16)
            for dst, src in ((wq, io["q_wT"]), (wk, io["k_wT"]), (w3[:, 0:D], io["v_wT"]), (w3[:, D:D + E], io["gate_wT"]),
                             (w3[:, D + E:W3], io["lora_AT"]), (qb, io["q_b"]), (kb, io["k_b"])):
                sp.dma_start(dst if isinstance(dst, bass.AP) else dst[:], src).then_inc(w_loaded, 16)
            sp.dma_start(vb_row[:], io["v_b"].partition_broadcast(P)).then_inc(w_loaded, 16)
            sp.dma_start(gb_row[:], io["gate_b"].partition_broadcast(P)).then_inc(w_loaded, 16)
            sp.dma_start(bo_row[:], io["bo"].partition_broadcast(P)).then_inc(w_loaded, 16)
            sp.dma_start(ob_row[:], io["out_b"].partition_broadcast(P)).then_inc(w_loaded, 16)
            sp.dma_start(x[:, GT:, :], io["x"][:, GT:, :]).then_inc(x_rest, 16)
            sp.dma_start(wi[:], io["wiT"]).then_inc(w_loaded, 16)
            sp.dma_start(bi[:], io["bi"]).then_inc(w_loaded, 16)
            sp.dma_start(lora_b[:], io["lora_BT"]).then_inc(w_loaded, 16)
            sp.dma_start(wo[:], io["woT"]).then_inc(w_loaded, 16)
            with sp.Fori(0, NG) as g:
                sp.wait_ge(parts_ready, g + 1)
                sp.sem_inc(passed, 1)
                for qk in range(2):
                    dst = io["scratch"][qk, :, bass.ds(g // QC, 1), :, bass.ds(g % QC * G, G)]
                    sp.dma_start(dst.rearrange("s b c t -> c (b s) t"), parts[:, qk, :, :]).then_inc(parts_stored, 16)
            sp.wait_ge(parts_stored, 32 * NG)

        @block.gpsimd
        def _(pool):
            pool.memset(ident[:], 0.0).then_inc(consts, 1)
            pool.wait_ge(consts, 1)
            pool.affine_select(out=ident[:], in_=ident[:], compare_op=ALU.not_equal, fill=1.0, base=0,
                               pattern=[[-1, P]], channel_multiplier=1).then_inc(consts, 1)
            pool.memset(v_aug[:, :, :, DH:VW], 1.0).then_inc(consts, 1)
            pool.memset(minus_half[:], -0.5).then_inc(consts, 1)
            pool.memset(eps[:], EPS).then_inc(consts, 1)
            for e in range(E):
                pool.memset(rank_w[:, e:e + 1], float(E - e)).then_inc(consts, 1)
            pool.wait_ge(w_loaded, 16 * NW)
            pool.tensor_scalar(bo2_row[:], bo_row[:], 2.0, None, ALU.mult).then_inc(consts, 1)
            pool.tensor_scalar(qbs[:], qb[:], SCALE, None, ALU.mult).then_inc(consts, 1)

            def norm(g):
                pool.wait_ge(stats_ready, g + 1)
                pool.tensor_tensor(var_eps[:], mv[:, :, 1], eps[:], ALU.add).then_inc(pool_link, 1)
                pool.wait_ge(pool_link, g + 1)
                pool.tensor_tensor(rstd[:], var_eps[:], minus_half[:], ALU.pow).then_inc(rstd_ready, 1)

            def project(part, g, par, first, last):
                if part != 0:
                    return
                if first:
                    pool.wait_ge(x_first, 16)
                else:
                    pool.wait_ge(x_rest, 16)
                    pool.wait_ge(y_done, g)
                xg = x[:, bass.ds(g * GT, GT), :]
                pool.tensor_tensor(xob[par][:], xg, ob_row[:].unsqueeze(1).broadcast_to([P, GT, D]),
                                   ALU.add).then_inc(xob_ready, 1)
                if not last:
                    norm(g + 1)
                pool.wait_ge(raw_copied, 4 * g + 4)
                vdst = v_aug[:, bass.ds(g // QC * NHG, NHG), bass.ds(g % QC * GT * HG, GT * HG), 0:DH]
                for j in range(GT):
                    pool.tensor_tensor(vdst[:, :, j * HG:(j + 1) * HG, :],
                                       raw[:, j, 0:D].rearrange("p (u h d) -> p u h d", u=NHG, d=DH),
                                       vb_row[:].rearrange("p (u h d) -> p u h d", u=NHG, d=DH),
                                       ALU.add).then_inc(v_kept, 1)

            def experts(part, g, par):
                pass

            def masked(g, par, first, last):
                pass

            pool.wait_ge(consts, NCONST)
            norm(0)
            run(pool, schedule(project, experts, masked), experts)

        @block.vector
        def _(dve):
            chain = Chain(dve, dve_link)
            link = chain.link
            bc = lambda a, n=E: a.unsqueeze(2).broadcast_to([P, GT, n])

            def statistics(g, first=False):
                if first:
                    dve.wait_ge(x_first, 16)
                else:
                    dve.wait_ge(x_rest, 16)
                    dve.wait_ge(xnT_turned, g)
                for j in range(GT):
                    ins = dve.bn_stats(stats[:, j, :], x[:, bass.ds(g * GT + j, 1), :].rearrange("p a d -> p (a d)"))
                link(ins)
                dve.sem_inc(passed, 1)
                for j in range(GT):
                    ins = dve.bn_aggr(mv[:, j, :], stats[:, j, :])
                ins.then_inc(stats_ready, 1)

            def normalise(g):
                dve.wait_ge(rstd_ready, g + 1)
                for j in range(GT):
                    ins = dve.tensor_scalar(xn[:, j, :], x[:, bass.ds(g * GT + j, 1), :].rearrange("p a d -> p (a d)"),
                                            mv[:, j, 0:1], rstd[:, j:j + 1], ALU.subtract, ALU.mult)
                ins.then_inc(xn_ready, 1)

            ranks = rank_w[:].unsqueeze(1).broadcast_to([P, GT, E])

            def choose(src, best):
                link(dve.tensor_reduce(best[:], src[:], AX.X, ALU.max))
                link(dve.tensor_tensor(eq[:], src[:], bc(best[:]), ALU.is_equal))
                link(dve.tensor_tensor(eq[:], eq[:], ranks, ALU.mult))
                link(dve.tensor_reduce(wmax[:], eq[:], AX.X, ALU.max))

            def project(part, g, par, first, last):
                if part == 1:
                    dve.wait_ge(raw_copied, 4 * g + 4)
                    if first:
                        dve.wait_ge(consts, NCONST)
                    link(dve.tensor_tensor(lg[:], raw[:, :, D:D + E], gb_row[:].unsqueeze(1).broadcast_to([P, GT, E]), ALU.add))
                    link(dve.tensor_reduce(mx[:], lg[:], AX.X, ALU.max))
                    dve.tensor_tensor(lg[:], lg[:], bc(mx[:]), ALU.subtract).then_inc(lg_ready, 1)
                    if not last:
                        statistics(g + 1)
                elif part == 2:
                    dve.wait_ge(ex_ready, g + 1)
                    link(dve.tensor_reduce(sm[:], ex[:], AX.X, ALU.add))
                    link(dve.reciprocal(sm[:], sm[:]))
                    link(dve.tensor_tensor(sc[:], ex[:], bc(sm[:]), ALU.mult))
                    choose(sc, m1)
                    link(dve.tensor_tensor(mask[0][:], eq[:], bc(wmax[:]), ALU.is_equal))
                    link(dve.scalar_tensor_tensor(out=sc2[:], in0=mask[0][:], scalar=-2.0, in1=sc[:],
                                                  op0=ALU.mult, op1=ALU.add))
                    choose(sc2, m2)
                    link(dve.tensor_tensor(vs[par][:], m1[:], m2[:], ALU.add))
                    link(dve.tensor_tensor(eq[:], eq[:], bc(wmax[:]), ALU.is_equal))
                    link(dve.tensor_tensor(mask[1][:], eq[:], mask[0][:], ALU.subtract))
                    if not first:
                        dve.wait_ge(amT_turned, g)
                    for s in range(2):
                        am_op = dve.tensor_tensor(am[s][:].rearrange("p j (e r) -> p j e r", r=R),
                                                  raw[:, :, D + E:W3].rearrange("p j (e r) -> p j e r", r=R),
                                                  mask[s][:].unsqueeze(3).broadcast_to([P, GT, E, R]), ALU.mult)
                    am_op.then_inc(am_ready, 1)
                elif part == 3:
                    if not last:
                        normalise(g + 1)

            def experts(part, g, par):
                for f, s, n in hidden(part):
                    if s == 1:
                        dve.wait_ge(z_read, 8 * g + n + 2)
                        dve.tensor_tensor(hT[:, f, :], hs[f % 2][0][:], hs[f % 2][1][:], ALU.add).then_inc(h_added, 1)
                if part <= FC:
                    return
                dve.wait_ge(y_ps, g + 1)
                link(dve.tensor_tensor(y1[:], psY[:], bo2_row[:].unsqueeze(1).broadcast_to([P, GT, D]), ALU.add))
                link(dve.tensor_tensor(y2[:], y1[:], vs[par][:].unsqueeze(2).broadcast_to([P, GT, D]), ALU.mult))
                dve.wait_ge(xob_ready, g + 1)
                dve.tensor_tensor(y_tok[:, bass.ds(g * GT, GT), :], y2[:], xob[par][:], ALU.add).then_inc(y_done, 1)

            def masked(g, par, first, last):
                dve.wait_ge(hi_ready, g + 1)
                dve.tensor_tensor(rest[:], qk32[:], parts[:, :, 0, :], ALU.subtract).then_inc(rest_ready, 1)
                dve.wait_ge(mid_ready, g + 1)
                dve.tensor_tensor(parts[:, :, 2, :], rest[:], parts[:, :, 1, :], ALU.subtract).then_inc(parts_ready, 1)

            dve.sem_inc(h_added, 2)
            dve.sem_inc(y_done, 1)
            statistics(0, first=True)
            normalise(0)
            run(dve, schedule(project, experts, masked), experts, per_pair=2 * LINKS, chain=chain)

        @block.scalar
        def _(act):
            def project(part, g, par, first, last):
                if part == 0:
                    act.wait_ge(xnT_turned, g + 1)
                    if first:
                        act.wait_ge(consts, NCONST)
                        act.wait_ge(w_loaded, 16 * NW)
                    act.copy(xnT[par][:], psA[:]).then_inc(xnT_ready, 1)
                elif part == 1:
                    if not first:
                        act.wait_ge(v_kept, 4 * g)
                        act.wait_ge(am_ready, g)
                    for j in range(GT):
                        act.wait_ge(vga_ps, 4 * g + j + 1)
                        act.copy(raw[:, j, :], psV[:, j % 2, 0:W3]).then_inc(raw_copied, 1)
                elif part == 2:
                    act.wait_ge(lg_ready, g + 1)
                    act.activation(ex[:], lg[:], ACT.Exp).then_inc(ex_ready, 1)
                    act.wait_ge(qk_ps, g + 1)
                    if not first:
                        act.wait_ge(parts_ready, g)
                    act.activation(qk32[:, 0, :], psQK[:, 0, :], ACT.Identity, bias=qbs[:, 0:1], scale=SCALE)
                    act.activation(qk32[:, 1, :], psQK[:, 1, :], ACT.Identity, bias=kb[:, 0:1]).then_inc(qk32_ready, 1)
                elif part == 3:
                    act.wait_ge(qk32_ready, g + 1)
                    if not first:
                        act.wait_ge(parts_stored, 32 * g)
                    act.copy(parts[:, :, 0, :], qk32[:]).then_inc(hi_ready, 1)

            def experts(part, g, par):
                for f, s, n in hidden(part):
                    act.wait_ge(h_added, 4 * g + f + 1)
                    act.wait_ge(z_ready, 8 * g + n)
                    act.activation(hs[f % 2][s][:], psZ[:, f % 2, :], ACT.Relu, bias=bi[:, f:f + 1]).then_inc(z_read, 1)

            def masked(g, par, first, last):
                for s in range(2):
                    act.wait_ge(amT_turned, g + 1)
                    ins = act.copy(amT[par][s][:], psV[:, s, :])
                ins.then_inc(amT_ready, 1)
                act.wait_ge(rest_ready, g + 1)
                act.copy(parts[:, :, 1, :], rest[:]).then_inc(mid_ready, 1)

            act.sem_inc(z_read, 2)
            run(act, schedule(project, experts, masked), experts)

        @block.tensor
        def _(pe):
            def turn_x(g, first):
                pe.wait_ge(xn_ready, g + 1)
                if first:
                    pe.wait_ge(consts, NCONST)
                    pe.wait_ge(w_loaded, 16 * NW)
                else:
                    pe.wait_ge(xnT_ready, g)
                for j in range(GT):
                    mm = pe.transpose(psA[:, j * P:(j + 1) * P], xn[:, j, :], ident[:])
                mm.then_inc(xnT_turned, 1)

            def project(part, g, par, first, last):
                if part == 0:
                    turn_x(g, first)
                elif part == 1:
                    pe.wait_ge(xnT_ready, g + 1)
                    for j in range(GT):
                        if j < 2:
                            if not first:
                                pe.wait_ge(amT_ready, g)
                        else:
                            pe.wait_ge(raw_copied, 4 * g + j - 1)
                        pe.matmul(psV[:, j % 2, 0:W3], xnT[par][:, j * P:(j + 1) * P], w3[:],
                                  start=True, stop=True).then_inc(vga_ps, 1)
                elif part == 2:
                    if not first:
                        pe.wait_ge(hi_ready, g)
                    pe.matmul(psQK[:, 0, :], wq[:], xnT[par][:], start=True, stop=True)
                    pe.matmul(psQK[:, 1, :], wk[:], xnT[par][:], start=True, stop=True).then_inc(qk_ps, 1)

            def experts(part, g, par):
                if part == 0:
                    pe.wait_ge(amT_ready, g + 1)
                for f, s, n in hidden(part):
                    before = ORDER.index((f, 0)) + 1 if s else (ORDER.index((f - 2, 1)) + 1 if f >= 2 else f - 1)
                    pe.wait_ge(z_read, 8 * g + before + 2)
                    z, fs = psZ[:, f % 2, :], slice(f * P, (f + 1) * P)
                    if s == 0:
                        pe.matmul(z, wi[:, fs], xnT[par][:], start=True, stop=False, skip_group_check=True)
                    pe.matmul(z, lora_b[:, fs], amT[par][s][:], start=False, stop=(s == 1),
                              skip_group_check=True).then_inc(z_ready, 1)
                if part < FC:
                    return
                for f in range(2) if part == FC else range(2, FC):
                    pe.wait_ge(h_added, 4 * g + f + 1 + 2)
                    for j in range(GT):
                        mm = pe.matmul(psY[:, j, :], hT[:, f, j * P:(j + 1) * P], wo[:, f, :],
                                       start=(f == 0 and j == 0), stop=(f == FC - 1), skip_group_check=True)
                if part > FC:
                    mm.then_inc(y_ps, 1)

            def masked(g, par, first, last):
                pe.wait_ge(am_ready, g + 1)
                pe.wait_ge(raw_copied, 4 * g + 4)
                for s in range(2):
                    for j in range(GT):
                        mm = pe.transpose(psV[:, s, j * P:(j + 1) * P], am[s][:, j, :], ident[:])
                mm.then_inc(amT_turned, 1)

            run(pe, schedule(project, experts, masked), experts)


def attention_block(nc, io, keep):
    with ExitStack() as ctx:
        sb = lambda name, shape, dt=F32: ctx.enter_context(nc.sbuf_tensor(name, shape, dt))
        ps = lambda name, shape: ctx.enter_context(nc.psum_tensor(name, shape, F32))
        sem = lambda name: ctx.enter_context(nc.semaphore(name))

        ident, v_aug, ctx_tok = keep["ident"], keep["v_aug"], keep["ctx_tok"]
        kM, kE = ([sb(f"{n}{i}", [P, 2, S], BF16) for i in range(2)] for n in ("kM", "kE"))
        qM, qE = ([sb(f"{n}{i}", [P, 2, 2, G], BF16) for i in range(2)] for n in ("qM", "qE"))
        v = [sb(f"v{i}", [P, TILES * VW]) for i in range(2)]
        probs = sb("probs", [P, 2, HG, G])
        pmax = sb("pmax", [P, 2, 2, GT, KC])
        negmax = sb("negmax", [P, P])
        m_rest = sb("m_rest", [4 * GT, 2, P])
        m_parts = sb("m_parts", [4 * GT, NPART, P], BF16)
        acc_sb = sb("acc_sb", [P, G])
        rden = sb("rden", [P, GT * HG])

        psE = ps("psE", [P, 2, G])
        psM = ps("psM", [P, 2, 2, G])
        psO = ps("psO", [P, G])
        psT = ps("psT", [P, GT, P])

        ones_set = sem("ones_set")
        m_loaded = [sem("m_loaded0"), sem("m_loaded1")]
        e_loaded, rows_loaded = sem("e_loaded"), sem("rows_loaded")
        scores_ready, exp_done, pv_done = sem("scores_ready"), sem("exp_done"), sem("pv_done")
        m_ready, m_done = sem("m_ready"), sem("m_done")
        negmax_ready, negmax_turned, rows_ready, rows_step = (
            sem("negmax_ready"), sem("negmax_turned"), sem("rows_ready"), sem("rows_step"))
        acc_saved, ctx_turned, rden_ready, ctx_done = sem("acc_saved"), sem("ctx_turned"), sem("rden_ready"), sem("ctx_done")
        neg_set, passed = sem("neg_set"), sem("passed")
        NLOAD = 2 * 2 * NSLOT
        NCOPY = 5

        TURN = KT - LEAD + 2

        def chunk_steps(c, par, step, maxima=2, exp_chunk=True, last=False):
            for p in range(1, KT + 1):
                cc, kt, cpar = (c, p, par) if p < KT else (c + 1, 0, 1 - par)
                m = p - 1 + LEAD
                mx = (c + 1, m, 1 - par) if m < KT else (c + 2, m - KT, par)
                if maxima < (1 if m < KT else 2):
                    mx = None
                with_scores = (exp_chunk or p == KT) and not (last and p == KT)
                step(c, par, cc, kt, cpar, with_scores, mx, exp_chunk, p == TURN and maxima >= 1, maxima)

        def all_chunks(engine, step):
            for g in range(LEAD):
                step(-1, 1, -1, -1, 1, False, (0, g, 0), False, False, 2)
            chunk_steps(-1, 1, step, exp_chunk=False)
            with engine.Fori(0, (NCH - 2) // 2) as i:
                chunk_steps(2 * i, 0, step)
                chunk_steps(2 * i + 1, 1, step)
            chunk_steps(NCH - 2, 0, step, maxima=1)
            chunk_steps(NCH - 1, 1, step, maxima=0, last=True)

        block = ctx.enter_context(nc.Block())

        @block.sync
        def _(sp):
            def load_m(c, par):
                unit, qc = c // QC, c % QC
                for sc, dst, which, cols in ((io["scratch"][0], qM, Q_PART, G), (io["scratch"][1], kM, K_PART, S)):
                    for slot in range(NSLOT):
                        src = sc[which[slot]].rearrange("b (u j k d) t -> (b u) k d j t", u=NHG, j=2, k=2)
                        for jj in range(2):
                            part = src[bass.ds(unit, 1), jj, :, :, bass.ds(qc * G, G) if cols == G else slice(0, S)]
                            r = 64 * jj + DH * slot
                            sp.dma_start(dst[par][r:r + DH, jj, :, :] if cols == G else dst[par][r:r + DH, :, :], part.rearrange("a d j t -> (a d) j t")).then_inc(m_loaded[par], 16)

            def copy_e(c, par):
                for jj in range(2):
                    rows = slice(64 * jj, 64 * jj + DOTS)
                    sp.dma_start(kE[par][rows, :, :], kM[par][rows, :, :]).then_inc(e_loaded, 16)
                    sp.dma_start(qE[par][rows, jj, :, :], qM[par][rows, jj, :, :]).then_inc(e_loaded, 16)
                sp.dma_start(v[par][:], v_aug[:, bass.ds(c // QC, 1), :, :].rearrange("p u n w -> p (u n w)")).then_inc(e_loaded, 16)

            def load_rows(par):
                for jj in range(2):
                    for n in range(NPART):
                        r = 64 * jj + DOTS + n
                        sp.dma_start(qE[par][r:r + 1, jj, :, :].rearrange("p j (t q) -> p (j t) q", q=P),
                                     m_parts[2 * GT * jj:2 * GT * (jj + 1), n, :]).then_inc(rows_loaded, 16)

            def chunk(c, par, load=True):
                sp.wait_ge(scores_ready, TILES * c + 1)
                sp.sem_inc(passed, 1)
                sp.wait_ge(pv_done, KT * c + 2)
                sp.sem_inc(passed, 1)
                copy_e(c + 1, 1 - par)
                sp.wait_ge(rows_ready, c + 2)
                load_rows(1 - par)
                if load:
                    sp.wait_ge(e_loaded, 16 * NCOPY * (c + 2))
                    sp.sem_inc(passed, 1)
                    sp.wait_ge(m_ready, MAXOPS * (c + 2))
                    sp.sem_inc(passed, 1)
                    load_m((c + 3) % NCH, 1 - par)

            sp.wait_ge(ones_set, 2)
            load_m(0, 0)
            load_m(1, 1)
            sp.wait_ge(m_loaded[0], 16 * NLOAD)
            copy_e(0, 0)
            sp.wait_ge(rows_ready, 1)
            load_rows(0)
            sp.wait_ge(e_loaded, 16 * NCOPY)
            sp.wait_ge(m_ready, MAXOPS)
            load_m(2, 0)
            with sp.Fori(0, (NCH - 2) // 2) as i:
                chunk(2 * i, 0)
                chunk(2 * i + 1, 1)
            chunk(NCH - 2, 0, load=False)
            sp.wait_ge(m_loaded[0], 16 * NLOAD * (NCH // 2 + 1))

        @block.gpsimd
        def _(pool):
            for t in kM + kE:
                ins = pool.memset(t[:], 1.0)
            ins.then_inc(ones_set, 1)
            pool.wait_ge(ones_set, 1)
            for t in qM + qE:
                ins = pool.memset(t[:], 0.0)
            ins.then_inc(ones_set, 1)

        @block.tensor
        def _(pe):
            def max_scores(mc, mg, mpar, h, jj):
                op = MAXOPS * mc + 2 * mg + h
                n = 2 * mg + h
                j2, qt, kc = n // (GT * KC), n // KC % GT, n % KC
                if n == 0 and jj == 0:
                    pe.wait_ge(m_loaded[mpar], (mc // 2 + 1) * (16 * NLOAD))
                if jj == 0:
                    pe.wait_ge(m_done, op + 1)
                mm = pe.matmul(psM[:, h, jj, :], qM[mpar][:, jj, j2, qt * P:(qt + 1) * P],
                               kM[mpar][:, j2, kc * G:(kc + 1) * G], start=True, stop=True)
                if jj == 1:
                    mm.then_inc(m_ready, 1)

            def scores(cc, kt, cpar, j2, jj):
                if kt == 0 and j2 == 0 and jj == 0:
                    pe.wait_ge(e_loaded, (cc + 1) * (16 * NCOPY))
                    pe.wait_ge(rows_loaded, (cc + 1) * (16 * 2 * NPART))
                pe.wait_ge(exp_done, TILES * cc + HG * kt + 2 * j2 + jj + 1)
                pe.matmul(psE[:, jj, :], kE[cpar][:, j2, kt * P:(kt + 1) * P], qE[cpar][:, jj, j2, :],
                          start=True, stop=True).then_inc(scores_ready, 1)

            def products(c, kt, par):
                if kt == 0:
                    pe.wait_ge(acc_saved, c + 1)
                pe.wait_ge(exp_done, TILES * c + HG * (kt + 1) + 2)
                for g in range(HG):
                    mm = pe.matmul(psO[32 * g:32 * g + VW, :], v[par][:, (HG * kt + g) * VW:(HG * kt + g + 1) * VW],
                                   probs[:, kt % 2, g, :], start=(kt == 0), stop=(kt == KT - 1))
                mm.then_inc(pv_done, 1)

            def step(c, par, cc, kt, cpar, with_scores, mx, exp_chunk, turn, maxima):
                for j2 in range(2):
                    for jj in range(2):
                        if with_scores:
                            scores(cc, kt, cpar, j2, jj)
                    if j2 == 0 and exp_chunk:
                        products(c, (kt - 1) % KT, par)
                if mx:
                    for h in range(2):
                        for jj in range(2):
                            max_scores(*mx, h, jj)
                if turn:
                    pe.wait_ge(negmax_ready, c + 2)
                    if exp_chunk:
                        pe.wait_ge(ctx_done, c + 1)
                    pe.transpose(psT[:, 0, :], negmax[:], ident[:]).then_inc(negmax_turned, 1)
                if exp_chunk and kt == 0:
                    pe.wait_ge(acc_saved, c + 2)
                    if maxima >= 1:
                        pe.wait_ge(rows_ready, c + 2)
                    else:
                        pe.wait_ge(ctx_done, c + 1)
                    for j in range(GT):
                        tr = pe.transpose(psT[:, j, :], acc_sb[:, j * P:(j + 1) * P], ident[:])
                    tr.then_inc(ctx_turned, 1)

            pe.sem_inc(pv_done, 2)
            pe.sem_inc(ctx_turned, 1)
            all_chunks(pe, step)

        @block.scalar
        def _(act):
            def step(c, par, cc, kt, cpar, with_scores, mx, exp_chunk, turn, maxima):
                for j2 in range(2):
                    if with_scores:
                        if j2 == 0:
                            act.wait_ge(pv_done, KT * cc + kt + 1)
                        for jj in range(2):
                            n = TILES * cc + HG * kt + 2 * j2 + jj
                            act.wait_ge(scores_ready, n + 1)
                            act.activation(probs[:, kt % 2, 2 * j2 + jj, :], psE[:, jj, :], ACT.Exp).then_inc(exp_done, 1)
                    if j2 == 0 and kt == 0 and exp_chunk:
                        act.wait_ge(pv_done, KT * (c + 1) + 2)
                        act.wait_ge(ctx_turned, c + 1)
                        act.copy(acc_sb[:], psO[:]).then_inc(acc_saved, 1)

            act.sem_inc(exp_done, 2)
            all_chunks(act, step)

        @block.vector
        def _(dve):
            def step(c, par, cc, kt, cpar, with_scores, mx, exp_chunk, turn, maxima):
                for h in range(2):
                    if not mx:
                        break
                    mc, mg, mpar = mx
                    n = 2 * mg + h
                    j2, qt, kc = n // (GT * KC), n // KC % GT, n % KC
                    dve.wait_ge(m_ready, MAXOPS * mc + n + 1)
                    if n == 0 and (exp_chunk or mc == 1):
                        dve.wait_ge(negmax_ready, mc)
                    dve.tensor_reduce(pmax[:, :, j2, qt, kc], psM[:, h, :, :], AX.X, ALU.max).then_inc(m_done, 1)
                if mx and mx[1] == KT - 1:
                    mc = mx[0]
                    dve.wait_ge(m_done, MAXOPS * (mc + 1) + 2)
                    if exp_chunk:
                        dve.wait_ge(negmax_turned, mc)
                    dve.tensor_reduce(negmax[:, 0:4 * GT].rearrange("p (a b) -> p a b", b=GT),
                                      pmax[:].rearrange("p i j t k -> p (i j) t k"), AX.X, ALU.max,
                                      negate=True).then_inc(negmax_ready, 1)
                if turn:
                    m, rows = c + 1, slice(0, 4 * GT)
                    dve.wait_ge(negmax_turned, m + 1)
                    if exp_chunk:
                        dve.wait_ge(rows_loaded, m * (16 * 2 * NPART))
                    dve.tensor_copy(m_parts[:, 0, :], psT[rows, 0, :]).then_inc(rows_step, 1)
                    dve.wait_ge(rows_step, 3 * m + 1)
                    dve.tensor_tensor(m_rest[:, 0, :], psT[rows, 0, :], m_parts[:, 0, :], ALU.subtract).then_inc(rows_step, 1)
                    dve.wait_ge(rows_step, 3 * m + 2)
                    dve.tensor_copy(m_parts[:, 1, :], m_rest[:, 0, :]).then_inc(rows_step, 1)
                    dve.wait_ge(rows_step, 3 * m + 3)
                    dve.tensor_tensor(m_parts[:, 2, :], m_rest[:, 0, :], m_parts[:, 1, :], ALU.subtract).then_inc(rows_ready, 1)
                if exp_chunk and kt == 0:
                    turned = psT[:].rearrange("p j (g w) -> p (j g) w", g=HG)
                    dve.wait_ge(ctx_turned, c + 2)
                    dve.reciprocal(rden[:].unsqueeze(2), turned[:, :, DH:VW]).then_inc(rden_ready, 1)
                    dve.wait_ge(rden_ready, c + 1)
                    dst = ctx_tok[:, bass.ds(c // QC, 1), bass.ds(c % QC * GT, GT), :]
                    dve.tensor_tensor(dst.rearrange("p u j (g d) -> p (u j) g d", g=HG),
                                      psT[:].rearrange("p j (g w) -> p j g w", g=HG)[:, :, :, 0:DH],
                                      rden[:].rearrange("p (j g) -> p j g", g=HG).unsqueeze(3).broadcast_to([P, GT, HG, DH]),
                                      ALU.mult).then_inc(ctx_done, 1)

            dve.memset(psO[:], 0.0).then_inc(acc_saved, 1)
            dve.memset(negmax[:], 0.0).then_inc(neg_set, 1)
            dve.wait_ge(neg_set, 1)
            dve.sem_inc(m_done, 2)
            dve.sem_inc(ctx_done, 1)
            all_chunks(dve, step)


def output_block(nc, io, keep):
    with ExitStack() as ctx:
        sb = lambda name, shape: ctx.enter_context(nc.sbuf_tensor(name, shape, F32))
        ps = lambda name, shape: ctx.enter_context(nc.psum_tensor(name, shape, F32))
        sem = lambda name: ctx.enter_context(nc.semaphore(name))
        ident, ctx_tok, y_tok = keep["ident"], keep["ctx_tok"], keep["y_tok"]
        out_w = sb("out_w", [P, D])
        ctx_g = [sb(f"ctx_g{i}", [P, GT, D]) for i in range(2)]
        ctxT = [sb(f"ctxT{i}", [P, G]) for i in range(2)]
        res = sb("res", [P, T // P, D])
        psC, psW = ps("psC", [P, 2, G]), ps("psW", [P, 2, GT, D])
        w_loaded, gathered, turned, copied, projected, added, stored = (
            sem(n) for n in ("w_loaded", "gathered", "turned", "copied", "projected", "added", "stored"))
        block = ctx.enter_context(nc.Block())

        @block.sync
        def _(sp):
            sp.dma_start(out_w[:], io["out_wT"]).then_inc(w_loaded, 16)
            for g in range(NG):
                sp.wait_ge(added, g + 1)
                sp.dma_start(io["out"][:, g * GT:(g + 1) * GT, :], res[:, g * GT:(g + 1) * GT, :]).then_inc(stored, 16)
            sp.wait_ge(stored, 16 * NG)

        @block.gpsimd
        def _(pool):
            for g in range(NG):
                if g >= 2:
                    pool.wait_ge(turned, g - 1)
                b, qc = g // QC, g % QC
                src = ctx_tok[:, b * NHG:(b + 1) * NHG, qc * GT:(qc + 1) * GT, :].rearrange("p u j e -> p j u e")
                pool.tensor_copy(ctx_g[g % 2][:].rearrange("p j (u e) -> p j u e", u=NHG), src).then_inc(gathered, 1)

        @block.tensor
        def _(pe):
            def project(g):
                pe.wait_ge(copied, g + 1)
                if g >= 2:
                    pe.wait_ge(added, g - 1)
                for j in range(GT):
                    mm = pe.matmul(psW[:, g % 2, j, :], ctxT[g % 2][:, j * P:(j + 1) * P], out_w[:], start=True, stop=True)
                mm.then_inc(projected, 1)

            pe.wait_ge(w_loaded, 16)
            for g in range(NG):
                pe.wait_ge(gathered, g + 1)
                if g >= 2:
                    pe.wait_ge(copied, g - 1)
                for j in range(GT):
                    tr = pe.transpose(psC[:, g % 2, j * P:(j + 1) * P], ctx_g[g % 2][:, j, :], ident[:])
                tr.then_inc(turned, 1)
                if g >= 1:
                    project(g - 1)
            project(NG - 1)

        @block.scalar
        def _(act):
            for g in range(NG):
                act.wait_ge(turned, g + 1)
                if g >= 2:
                    act.wait_ge(projected, g - 1)
                act.copy(ctxT[g % 2][:], psC[:, g % 2, :]).then_inc(copied, 1)

        @block.vector
        def _(dve):
            for g in range(NG):
                dve.wait_ge(projected, g + 1)
                dve.tensor_tensor(res[:, g * GT:(g + 1) * GT, :], psW[:, g % 2, :, :],
                                  y_tok[:, g * GT:(g + 1) * GT, :], ALU.add).then_inc(added, 1)


def build(nc, io):
    with ExitStack() as ctx:
        sb = lambda name, shape: ctx.enter_context(nc.sbuf_tensor(name, shape, F32))
        keep = {
            "ident": sb("ident", [P, P]),
            "y_tok": sb("y_tok", [P, T // P, D]),
            "ctx_tok": sb("ctx_tok", [P, B * NHG, QC * GT, HG * DH]),
        }
        with ExitStack() as inner:
            isb = lambda name, shape: inner.enter_context(nc.sbuf_tensor(name, shape, F32))
            keep["v_aug"] = isb("v_aug", [P, B * NHG, TILES, VW])
            with nc.sbuf_tensor("x", [P, T // P, D], F32) as x:
                keep["x"] = x
                tokens_block(nc, io, keep)
            attention_block(nc, io, keep)
        output_block(nc, io, keep)


def kernel(L0_attn_query, L0_attn_mask, L0_attn_q_w, L0_attn_q_b, L0_attn_k_w, L0_attn_k_b, L0_attn_v_w, L0_attn_v_b,
           L0_attn_out_w, L0_attn_out_b, L0_ffn_wi, L0_ffn_bi, L0_ffn_wo, L0_ffn_bo, L0_ffn_lora_A, L0_ffn_lora_B,
           L0_ffn_gate_w, L0_ffn_gate_b):
    import numpy as np
    import concourse.bacc as bacc
    from concourse.bass_utils import run_bass_kernel_spmd

    c = np.ascontiguousarray
    lay = {
        "x": c(np.asarray(L0_attn_query)),
        "q_wT": c(np.asarray(L0_attn_q_w).T), "k_wT": c(np.asarray(L0_attn_k_w).T),
        "v_wT": c(np.asarray(L0_attn_v_w).T), "out_wT": c(np.asarray(L0_attn_out_w).T),
        "q_b": c(L0_attn_q_b), "k_b": c(L0_attn_k_b), "v_b": c(L0_attn_v_b), "out_b": c(L0_attn_out_b),
        "gate_wT": c(np.asarray(L0_ffn_gate_w).T), "gate_b": c(L0_ffn_gate_b),
        "wiT": c(np.asarray(L0_ffn_wi).T), "bi": c(np.asarray(L0_ffn_bi).reshape(FC, P).T), "woT": c(np.asarray(L0_ffn_wo).T), "bo": c(L0_ffn_bo),
        "lora_AT": c(np.asarray(L0_ffn_lora_A).reshape(E * R, D).T),
        "lora_BT": c(np.asarray(L0_ffn_lora_B).transpose(0, 2, 1).reshape(E * R, F)),
    }
    nc = bacc.Bacc("TRN2", target_bir_lowering=False, num_devices=1)
    io = {n: nc.dram_tensor(f"in_{n}", a.shape, F32, kind="ExternalInput").ap() for n, a in lay.items()}
    out = nc.dram_tensor("out", (B, S, D), F32, kind="ExternalOutput").ap()
    io["x"] = io["x"].rearrange("b (n p) d -> p (b n) d", p=P)
    io["out"] = out.rearrange("b (n p) d -> p (b n) d", p=P)
    io["woT"] = io["woT"].rearrange("(f p) d -> p f d", p=P)
    io["q_b"] = io["q_b"].unsqueeze(1)
    io["k_b"] = io["k_b"].unsqueeze(1)
    io["scratch"] = nc.dram_tensor("qk_parts", (2, NPART, B, D, S), BF16, kind="Internal").ap()
    build(nc, io)
    r = run_bass_kernel_spmd(nc, [{f"in_{n}": a for n, a in lay.items()}], core_ids=[0])
    return r.results[0]["out"]
```

```python
from contextlib import ExitStack

import concourse.bass as bass
from concourse import mybir

F32 = mybir.dt.float32
BF16 = mybir.dt.bfloat16
ALU = mybir.AluOpType
ACT = mybir.ActivationFunctionType
AX = mybir.AxisListType

P = 128
D = 128
H = 16
DH = D // H
B = 2
S = 2048
T = B * S
E, R = 8, 16
F = 512
FC = F // P
G = 512
GT = G // P
NG = T // G
EPS = 1e-5
SCALE = float(DH) ** -0.5

NPART = 3
Q_PART = (0, 0, 0, 1, 1, 2)
K_PART = (0, 1, 2, 0, 1, 0)
NSLOT = len(Q_PART)
DOTS = NSLOT * DH
HG = 4
NHG = H // HG
QC = S // G
NCH = B * NHG * QC
KT = S // P
KC = S // G
TILES = KT * HG
MAXOPS = 2 * KT
LEAD = 7
VW = DH + 1
W3 = D + E + E * R
LINKS = 21


class Chain:

    def __init__(self, engine, sem):
        self.engine, self.sem, self.base, self.n = engine, sem, 0, 0

    def link(self, ins):
        self.n += 1
        ins.then_inc(self.sem, 1)
        self.engine.wait_ge(self.sem, self.base + self.n)


def program(nc, io):
    with ExitStack() as ctx:
        sb = lambda name, shape, dt=F32: ctx.enter_context(nc.sbuf_tensor(name, shape, dt))
        ps = lambda name, shape: ctx.enter_context(nc.psum_tensor(name, shape, F32))
        sem = lambda name: ctx.enter_context(nc.semaphore(name))

        ident = sb("ident", [P, P])
        y_tok = sb("y_tok", [P, T // P, D])
        v_aug = sb("v_aug", [P, B * NHG, TILES, VW])
        x = sb("x", [P, T // P, D])
        probs = sb("probs", [P, 2, HG, G])
        psE = ps("psE", [P, 2, G])
        psM = ps("psM", [P, 2, 2, G])
        psO = ps("psO", [P, G])
        psT = ps("psT", [P, GT, P])
        wq, wk = sb("wq", [P, D]), sb("wk", [P, D])
        w3 = sb("w3", [P, W3])
        wi, lora_b, wo = sb("wi", [P, F]), sb("lora_b", [P, F]), sb("wo", [P, FC, D])
        qb, kb, qbs, bi = sb("qb", [P, 1]), sb("kb", [P, 1]), sb("qbs", [P, 1]), sb("bi", [P, FC])
        vb_row, gb_row, bo_row, ob_row = sb("vb_row", [P, D]), sb("gb_row", [P, E]), sb("bo_row", [P, D]), sb("ob_row", [P, D])
        bo2_row, rank_w = sb("bo2_row", [P, D]), sb("rank_w", [P, E])
        stats, mv, rstd = sb("stats", [P, GT, 6]), sb("mv", [P, GT, 2]), sb("rstd", [P, GT])
        var_eps, eps, minus_half = sb("var_eps", [P, GT]), sb("eps", [P, GT]), sb("minus_half", [P, GT])
        xn = sb("xn", [P, GT, D])
        xnT = [sb(f"xnT{i}", [P, G]) for i in range(2)]
        qk32, rest = sb("qk32", [P, 2, G]), sb("rest", [P, 2, G])
        parts = sb("parts", [P, 2, NPART, G], BF16)
        raw = sb("raw", [P, GT, W3])
        lg, ex, sc, sc2, eq = (sb(n, [P, GT, E]) for n in ("lg", "ex", "sc", "sc2", "eq"))
        mask = [sb(f"mask{s}", [P, GT, E]) for s in range(2)]
        mx, sm, m1, m2, wmax = (sb(n, [P, GT]) for n in ("mx", "sm", "m1", "m2", "wmax"))
        vs = [sb(f"vs{i}", [P, GT]) for i in range(2)]
        am = [sb(f"am{s}", [P, GT, E * R]) for s in range(2)]
        amT = [[sb(f"amT{i}{s}", [P, G]) for s in range(2)] for i in range(2)]
        xob = [sb(f"xob{i}", [P, GT, D]) for i in range(2)]
        hT = probs[:, 0, :, :]
        hs = [[probs[:, 1, 2 * f + s, :] for s in range(2)] for f in range(2)]
        y1, y2 = sb("y1", [P, GT, D]), sb("y2", [P, GT, D])

        psA = psT[:].rearrange("p j q -> p (j q)")
        psQK, psV, psZ = psM[:, 0, :, :], psM[:, 1, :, :], psE[:]
        psY = psO[:].rearrange("p (j d) -> p j d", j=GT)

        x_first, x_rest, w_loaded, w_rest = sem("x_first"), sem("x_rest"), sem("w_loaded"), sem("w_rest")
        consts, scaled = sem("consts"), sem("scaled")
        stats_ready, rstd_ready, xn_ready = sem("stats_ready"), sem("rstd_ready"), sem("xn_ready")
        xnT_turned, xnT_ready, qk_ps = sem("xnT_turned"), sem("xnT_ready"), sem("qk_ps")
        qk32_ready, hi_ready, rest_ready, mid_ready, parts_ready = (
            sem("qk32_ready"), sem("hi_ready"), sem("rest_ready"), sem("mid_ready"), sem("parts_ready"))
        parts_stored = sem("parts_stored")
        vga_ps, raw_copied, lg_ready, ex_ready, masks_ready = (
            sem("vga_ps"), sem("raw_copied"), sem("lg_ready"), sem("ex_ready"), sem("masks_ready"))
        v_kept, xob_ready, am_ready, amT_turned, amT_ready = (
            sem("v_kept"), sem("xob_ready"), sem("am_ready"), sem("amT_turned"), sem("amT_ready"))
        z_ready, z_read, h_added, y_ps, y_done = sem("z_ready"), sem("z_read"), sem("h_added"), sem("y_ps"), sem("y_done")
        dve_link, pool_link = sem("dve_link"), sem("pool_link")
        passed = sem("passed")
        NW = 11
        NCONST = 5 + E

        def hidden(part):
            if part > FC:
                return []
            pieces = [(part, 0)] * (part < FC) + [(part - 1, 1)] * (part > 0)
            return [(f, s, ORDER.index((f, s)) + 1) for f, s in pieces]

        ORDER = [(0, 0)] + [x for f in range(1, FC) for x in ((f, 0), (f - 1, 1))] + [(FC - 1, 1)]

        def schedule(project, experts, masked):
            def step(g, par, first=False, last=False):
                for part in range(FC):
                    if not first:
                        experts(part, g - 1, 1 - par)
                    project(part, g, par, first, last)
                if not first:
                    experts(FC, g - 1, 1 - par)
                masked(g, par, first, last)
                if not first:
                    experts(FC + 1, g - 1, 1 - par)
            return step

        def run(engine, step, per_pair=0, chain=None):
            step(0, 0, first=True)
            base = chain.n if chain else 0
            with engine.Fori(0, (NG - 2) // 2) as i:
                if chain:
                    chain.base, chain.n = i * per_pair + base, 0
                step(2 * i + 1, 1)
                step(2 * i + 2, 0)
            if chain:
                assert chain.n == per_pair, chain.n
                chain.base, chain.n = base + per_pair * ((NG - 2) // 2), 0
            step(NG - 1, 1, last=True)

        ctx_tok = x[:].rearrange("p n d -> p (n d)").rearrange("p (t w) -> p t w", w=HG * DH)
        kM, kE = ([sb(f"{n}{i}", [P, 2, S], BF16) for i in range(2)] for n in ("kM", "kE"))
        qM, qE = ([sb(f"{n}{i}", [P, 2, 2, G], BF16) for i in range(2)] for n in ("qM", "qE"))
        v = [sb(f"v{i}", [P, TILES * VW]) for i in range(2)]
        pmax = [sb(f"pmax{i}", [P, 2, 2, GT, KC]) for i in range(2)]
        negmax = sb("negmax", [P, P])
        m_rest = sb("m_rest", [4 * GT, 2, P])
        m_parts = sb("m_parts", [4 * GT, NPART, P], BF16)
        acc_sb = sb("acc_sb", [P, G])
        rden = sb("rden", [P, GT * HG])

        ones_set, spread = sem("ones_set"), sem("spread")
        m_loaded = [sem("m_loaded0"), sem("m_loaded1")]
        e_loaded, rows_loaded = sem("e_loaded"), sem("rows_loaded")
        scores_ready, exp_done, pv_done = sem("scores_ready"), sem("exp_done"), sem("pv_done")
        m_ready, m_done = sem("m_ready"), sem("m_done")
        negmax_ready, negmax_turned, rows_ready, rows_step = (
            sem("negmax_ready"), sem("negmax_turned"), sem("rows_ready"), sem("rows_step"))
        acc_saved, ctx_turned, rden_ready, ctx_done = sem("acc_saved"), sem("ctx_turned"), sem("rden_ready"), sem("ctx_done")
        neg_set = sem("neg_set")
        NROWS = 2 * NPART
        NLOAD = 2 * 2 * NSLOT
        NCOPY = 5

        COLLECT = KT - LEAD + 1

        def chunk_steps(c, par, step, chunks_left=2, exp_chunk=True, last=False, beside=None):
            def maxima(p):
                ahead, m = divmod(p - 1 + LEAD, KT)
                return (c + 1 + ahead, m, (par + 1 + ahead) % 2) if chunks_left > ahead else None

            for p in range(1, KT + 1):
                cc, kt, cpar = (c, p, par) if p < KT else (c + 1, 0, 1 - par)
                step(c, par, cc, kt, cpar, (exp_chunk or p == KT) and not (last and p == KT), maxima(p), exp_chunk,
                     since=p - COLLECT if chunks_left > 0 else -1,
                     wide=0 if chunks_left > 1 else (p - COLLECT if chunks_left else KT))
                if beside:
                    beside(p)

        def score_bank(j2, jj, wide):
            return psM[:, 0, jj, :] if wide > 0 and j2 == 1 else psE[:, jj, :]

        def all_chunks(engine, step, experts, output, lag=0):
            def last_experts(p):
                part, rest_steps = divmod(p + LEAD - 1 - lag, 2)
                if rest_steps == 0 and 0 <= part < FC + 2:
                    experts(part, NG - 1, 1)

            for g in range(LEAD):
                step(-1, 1, -1, -1, 1, False, (0, g, 0), False)
                last_experts(g + 1 - LEAD)
            chunk_steps(-1, 1, step, exp_chunk=False, beside=last_experts)
            with engine.Fori(0, (NCH - 2) // 2) as i:
                chunk_steps(2 * i, 0, step)
                chunk_steps(2 * i + 1, 1, step)
            chunk_steps(NCH - 2, 0, step, chunks_left=1)
            chunk_steps(NCH - 1, 1, step, chunks_left=0, last=True,
                        beside=lambda p: output((p - 1) // 2, (p - 1) // 2 < NG - 1) if p % 2 else None)
            output(NG - 1, True, False)
            output(NG, False)

        out_w = sb("out_w", [P, D])
        ctx_g = [sb(f"ctx_g{i}", [P, GT, D]) for i in range(2)]
        ctxT = [sb(f"ctxT{i}", [P, G]) for i in range(2)]
        psC = psM[:, 1, 0, :]
        psW = psM[:, 1, 1, :].rearrange("p (j d) -> p j d", j=GT)
        gathered, turned, copied, projected, added, stored = (
            sem(n) for n in ("gathered", "turned", "copied", "projected", "added", "stored"))

        def last_chunk(g):
            return (g // QC * NHG + NHG - 1) * QC + g % QC

        def heads_of(g):
            b, qc = g // QC, g % QC
            src = ctx_tok.rearrange("p (u t) w -> p u t w", u=B * NHG)[:, b * NHG:(b + 1) * NHG, qc * GT:(qc + 1) * GT, :]
            return src.rearrange("p u j e -> p j u e")

        block = ctx.enter_context(nc.Block())

        @block.sync
        def _(sp):
            sp.dma_start(x[:, 0:GT, :], io["x"][:, 0:GT, :]).then_inc(x_first, 16)
            for dst, src in ((w3[:, 0:D], io["v_wT"]), (w3[:, D:D + E], io["gate_wT"]), (w3[:, D + E:W3], io["lora_AT"]),
                             (gb_row[:], io["gate_b"].partition_broadcast(P)), (wq[:], io["q_wT"]), (wk[:], io["k_wT"]),
                             (qb[:], io["q_b"]), (kb[:], io["k_b"]), (vb_row[:], io["v_b"].partition_broadcast(P)),
                             (bo_row[:], io["bo"].partition_broadcast(P)), (ob_row[:], io["out_b"].partition_broadcast(P))):
                sp.dma_start(dst, src).then_inc(w_loaded, 16)
            sp.dma_start(x[:, GT:, :], io["x"][:, GT:, :]).then_inc(x_rest, 16)
            for dst, src in ((bi[:], io["bi"]), (wi[:], io["wiT"]), (lora_b[:], io["lora_BT"]), (wo[:], io["woT"]),
                             (out_w[:], io["out_wT"])):
                sp.dma_start(dst, src).then_inc(w_rest, 16)

            def store_parts(first, end):
                with sp.Fori(first, end) as g:
                    sp.wait_ge(parts_ready, g + 1)
                    sp.sem_inc(passed, 1)
                    for qk in range(2):
                        dst = io["scratch"][qk, :, bass.ds(g // QC, 1), :, bass.ds(g % QC * G, G)]
                        sp.dma_start(dst.rearrange("s b c t -> c (b s) t"), parts[:, qk, :, :]).then_inc(parts_stored, 16)

            def load_m(c, par):
                unit, qc = c // QC, c % QC
                for sc, dst, which, cols in ((io["scratch"][0], qM, Q_PART, G), (io["scratch"][1], kM, K_PART, S)):
                    for slot in range(NSLOT):
                        src = sc[which[slot]].rearrange("b (u j k d) t -> (b u) k d j t", u=NHG, j=2, k=2)
                        for jj in range(2):
                            part = src[bass.ds(unit, 1), jj, :, :, bass.ds(qc * G, G) if cols == G else slice(0, S)]
                            r = 64 * jj + DH * slot
                            sp.dma_start(dst[par][r:r + DH, jj, :, :] if cols == G else dst[par][r:r + DH, :, :], part.rearrange("a d j t -> (a d) j t")).then_inc(m_loaded[par], 16)

            def copy_e(c, par):
                for jj in range(2):
                    rows = slice(64 * jj, 64 * jj + DOTS)
                    sp.dma_start(kE[par][rows, :, :], kM[par][rows, :, :]).then_inc(e_loaded, 16)
                    sp.dma_start(qE[par][rows, jj, :, :], qM[par][rows, jj, :, :]).then_inc(e_loaded, 16)
                sp.dma_start(v[par][:], v_aug[:, bass.ds(c // QC, 1), :, :].rearrange("p u n w -> p (u n w)")).then_inc(e_loaded, 16)

            def load_rows(par):
                for jj in range(2):
                    for n in range(NPART):
                        r = 64 * jj + DOTS + n
                        sp.dma_start(qE[par][r:r + 1, jj, :, :].rearrange("p j (t q) -> p (j t) q", q=P),
                                     m_parts[2 * GT * jj:2 * GT * (jj + 1), n, :]).then_inc(rows_loaded, 16)

            def chunk(c, par, load=True):
                sp.wait_ge(scores_ready, TILES * c + 1)
                sp.sem_inc(passed, 1)
                sp.wait_ge(pv_done, KT * c + 2)
                sp.sem_inc(passed, 1)
                copy_e(c + 1, 1 - par)
                sp.wait_ge(rows_ready, c + 2)
                load_rows(1 - par)
                if load:
                    sp.wait_ge(e_loaded, 16 * NCOPY * (c + 2))
                    sp.sem_inc(passed, 1)
                    sp.wait_ge(m_ready, MAXOPS * (c + 2))
                    sp.sem_inc(passed, 1)
                    load_m((c + 3) % NCH, 1 - par)

            store_parts(0, 2)
            sp.wait_ge(ones_set, 2)
            for src, others in ((kM[0], (kM[1], kE[0], kE[1])), (qM[0], (qM[1], qE[0], qE[1]))):
                for dst in others:
                    sp.dma_start(dst[:], src[:]).then_inc(spread, 16)
            store_parts(2, QC)
            sp.wait_ge(parts_stored, 32 * QC)
            sp.wait_ge(spread, 16 * 6)
            load_m(0, 0)
            store_parts(QC, QC + 1)
            load_m(1, 1)
            sp.wait_ge(m_loaded[0], 16 * NLOAD)
            sp.wait_ge(v_kept, GT * QC)
            copy_e(0, 0)
            store_parts(QC + 1, NG)
            sp.wait_ge(parts_stored, 32 * NG)
            sp.wait_ge(v_kept, GT * NG)
            sp.wait_ge(rows_ready, 1)
            load_rows(0)
            sp.wait_ge(e_loaded, 16 * NCOPY)
            sp.wait_ge(m_ready, MAXOPS)
            load_m(2, 0)
            with sp.Fori(0, (NCH - 2) // 2) as i:
                chunk(2 * i, 0)
                chunk(2 * i + 1, 1)
            chunk(NCH - 2, 0, load=False)
            sp.wait_ge(m_loaded[0], 16 * NLOAD * (NCH // 2 + 1))

            for g in range(NG):
                sp.wait_ge(added, g + 1)
                sp.dma_start(io["out"][:, g * GT:(g + 1) * GT, :], y_tok[:, g * GT:(g + 1) * GT, :]).then_inc(stored, 16)
            sp.wait_ge(stored, 16 * NG)

        @block.gpsimd
        def _(pool):
            pool.memset(ident[:], 0.0).then_inc(consts, 1)
            pool.wait_ge(consts, 1)
            pool.affine_select(out=ident[:], in_=ident[:], compare_op=ALU.not_equal, fill=1.0, base=0,
                               pattern=[[-1, P]], channel_multiplier=1).then_inc(consts, 1)
            pool.memset(v_aug[:, :, :, DH:VW], 1.0).then_inc(consts, 1)
            pool.memset(minus_half[:], -0.5).then_inc(consts, 1)
            pool.memset(eps[:], EPS).then_inc(consts, 1)
            for e in range(E):
                pool.memset(rank_w[:, e:e + 1], float(E - e)).then_inc(consts, 1)

            def norm(g):
                pool.wait_ge(stats_ready, g + 1)
                pool.tensor_tensor(var_eps[:], mv[:, :, 1], eps[:], ALU.add).then_inc(pool_link, 1)
                pool.wait_ge(pool_link, g + 1)
                pool.tensor_tensor(rstd[:], var_eps[:], minus_half[:], ALU.pow).then_inc(rstd_ready, 1)

            def project(part, g, par, first, last):
                if part != 0:
                    return
                if not last:
                    norm(g + 1)
                if not first:
                    pool.wait_ge(x_rest, 16)
                    pool.wait_ge(y_done, g)
                xg = x[:, bass.ds(g * GT, GT), :]
                pool.tensor_tensor(xob[par][:], xg, ob_row[:].unsqueeze(1).broadcast_to([P, GT, D]),
                                   ALU.add).then_inc(xob_ready, 1)
                pool.wait_ge(raw_copied, 4 * g + 4)
                vdst = v_aug[:, bass.ds(g // QC * NHG, NHG), bass.ds(g % QC * GT * HG, GT * HG), 0:DH]
                for j in range(GT):
                    pool.tensor_tensor(vdst[:, :, j * HG:(j + 1) * HG, :],
                                       raw[:, j, 0:D].rearrange("p (u h d) -> p u h d", u=NHG, d=DH),
                                       vb_row[:].rearrange("p (u h d) -> p u h d", u=NHG, d=DH),
                                       ALU.add).then_inc(v_kept, 1)

            def experts(part, g, par):
                pass

            def masked(g, par, first, last):
                if first:
                    pool.memset(kM[0][:], 1.0).then_inc(ones_set, 1)
                    pool.memset(qM[0][:], 0.0).then_inc(ones_set, 1)

            pool.wait_ge(consts, NCONST)
            norm(0)
            pool.wait_ge(w_loaded, 16 * NW)
            pool.tensor_scalar(bo2_row[:], bo_row[:], 2.0, None, ALU.mult).then_inc(scaled, 1)
            pool.tensor_scalar(qbs[:], qb[:], SCALE, None, ALU.mult).then_inc(scaled, 1)
            run(pool, schedule(project, experts, masked))

            for g in range(NG - 1):
                pool.wait_ge(ctx_done, last_chunk(g) + 2)
                if g >= 2:
                    pool.wait_ge(turned, g - 1)
                pool.tensor_copy(ctx_g[g % 2][:].rearrange("p j (u e) -> p j u e", u=NHG), heads_of(g)).then_inc(gathered, 1)

        @block.vector
        def _(dve):
            chain = Chain(dve, dve_link)
            link = chain.link
            bc = lambda a, n=E: a.unsqueeze(2).broadcast_to([P, GT, n])

            def statistics(g, first=False):
                if first:
                    dve.wait_ge(x_first, 16)
                else:
                    dve.wait_ge(x_rest, 16)
                    dve.wait_ge(xnT_turned, g)
                for j in range(GT):
                    ins = dve.bn_stats(stats[:, j, :], x[:, bass.ds(g * GT + j, 1), :].rearrange("p a d -> p (a d)"))
                link(ins)
                dve.sem_inc(passed, 1)
                for j in range(GT):
                    ins = dve.bn_aggr(mv[:, j, :], stats[:, j, :])
                ins.then_inc(stats_ready, 1)

            def normalise(g):
                dve.wait_ge(rstd_ready, g + 1)
                for j in range(GT):
                    ins = dve.tensor_scalar(xn[:, j, :], x[:, bass.ds(g * GT + j, 1), :].rearrange("p a d -> p (a d)"),
                                            mv[:, j, 0:1], rstd[:, j:j + 1], ALU.subtract, ALU.mult)
                ins.then_inc(xn_ready, 1)

            ranks = rank_w[:].unsqueeze(1).broadcast_to([P, GT, E])

            def choose(src, best):
                link(dve.tensor_reduce(best[:], src[:], AX.X, ALU.max))
                link(dve.tensor_tensor(eq[:], src[:], bc(best[:]), ALU.is_equal))
                link(dve.tensor_tensor(eq[:], eq[:], ranks, ALU.mult))
                link(dve.tensor_reduce(wmax[:], eq[:], AX.X, ALU.max))

            def project(part, g, par, first, last):
                if part == 1:
                    dve.wait_ge(raw_copied, 4 * g + 4)
                    if first:
                        dve.wait_ge(consts, NCONST)
                        dve.wait_ge(w_loaded, 16 * NW)
                        dve.wait_ge(scaled, 2)
                    link(dve.tensor_tensor(lg[:], raw[:, :, D:D + E], gb_row[:].unsqueeze(1).broadcast_to([P, GT, E]), ALU.add))
                    link(dve.tensor_reduce(mx[:], lg[:], AX.X, ALU.max))
                    dve.tensor_tensor(lg[:], lg[:], bc(mx[:]), ALU.subtract).then_inc(lg_ready, 1)
                    if not last:
                        statistics(g + 1)
                elif part == 2:
                    dve.wait_ge(ex_ready, g + 1)
                    link(dve.tensor_reduce(sm[:], ex[:], AX.X, ALU.add))
                    link(dve.reciprocal(sm[:], sm[:]))
                    link(dve.tensor_tensor(sc[:], ex[:], bc(sm[:]), ALU.mult))
                    choose(sc, m1)
                    link(dve.tensor_tensor(mask[0][:], eq[:], bc(wmax[:]), ALU.is_equal))
                    link(dve.scalar_tensor_tensor(out=sc2[:], in0=mask[0][:], scalar=-2.0, in1=sc[:],
                                                  op0=ALU.mult, op1=ALU.add))
                    choose(sc2, m2)
                    link(dve.tensor_tensor(vs[par][:], m1[:], m2[:], ALU.add))
                    link(dve.tensor_tensor(eq[:], eq[:], bc(wmax[:]), ALU.is_equal))
                    link(dve.tensor_tensor(mask[1][:], eq[:], mask[0][:], ALU.subtract))
                    if not first:
                        dve.wait_ge(amT_turned, g)
                    for s in range(2):
                        am_op = dve.tensor_tensor(am[s][:].rearrange("p j (e r) -> p j e r", r=R),
                                                  raw[:, :, D + E:W3].rearrange("p j (e r) -> p j e r", r=R),
                                                  mask[s][:].unsqueeze(3).broadcast_to([P, GT, E, R]), ALU.mult)
                    am_op.then_inc(am_ready, 1)
                elif part == 3:
                    if not last:
                        normalise(g + 1)

            def experts(part, g, par):
                for f, s, n in hidden(part):
                    if s == 1:
                        dve.wait_ge(z_read, 8 * g + n + 2)
                        dve.tensor_tensor(hT[:, f, :], hs[f % 2][0], hs[f % 2][1], ALU.add).then_inc(h_added, 1)
                if part <= FC:
                    return
                dve.wait_ge(y_ps, g + 1)
                link(dve.tensor_tensor(y1[:], psY, bo2_row[:].unsqueeze(1).broadcast_to([P, GT, D]), ALU.add))
                link(dve.tensor_tensor(y2[:], y1[:], vs[par][:].unsqueeze(2).broadcast_to([P, GT, D]), ALU.mult))
                dve.wait_ge(xob_ready, g + 1)
                dve.tensor_tensor(y_tok[:, bass.ds(g * GT, GT), :], y2[:], xob[par][:], ALU.add).then_inc(y_done, 1)

            def masked(g, par, first, last):
                dve.wait_ge(hi_ready, g + 1)
                dve.tensor_tensor(rest[:], qk32[:], parts[:, :, 0, :], ALU.subtract).then_inc(rest_ready, 1)
                dve.wait_ge(mid_ready, g + 1)
                dve.tensor_tensor(parts[:, :, 2, :], rest[:], parts[:, :, 1, :], ALU.subtract).then_inc(parts_ready, 1)

            dve.memset(negmax[:], 0.0).then_inc(neg_set, 1)
            dve.wait_ge(neg_set, 1)
            dve.sem_inc(m_done, 2)
            dve.sem_inc(ctx_done, 1)
            dve.sem_inc(h_added, 2)
            dve.sem_inc(y_done, 1)
            statistics(0, first=True)
            normalise(0)
            run(dve, schedule(project, experts, masked), per_pair=2 * LINKS, chain=chain)

            def cut(m, n, exp_chunk):
                turned = psT[0:4 * GT, 0, :]
                if n == 0:
                    dve.wait_ge(negmax_turned, m + 1)
                    if exp_chunk:
                        dve.wait_ge(rows_loaded, m * (16 * NROWS))
                    dve.tensor_copy(m_parts[:, 0, :], turned).then_inc(rows_step, 1)
                elif n == 1:
                    dve.wait_ge(rows_step, 3 * m + 1)
                    dve.tensor_tensor(m_rest[:, 0, :], turned, m_parts[:, 0, :], ALU.subtract).then_inc(rows_step, 1)
                elif n == 2:
                    dve.wait_ge(rows_step, 3 * m + 2)
                    dve.tensor_copy(m_parts[:, 1, :], m_rest[:, 0, :]).then_inc(rows_step, 1)
                else:
                    dve.wait_ge(rows_step, 3 * m + 3)
                    dve.tensor_tensor(m_parts[:, 2, :], m_rest[:, 0, :], m_parts[:, 1, :], ALU.subtract).then_inc(rows_ready, 1)

            def step(c, par, cc, kt, cpar, with_scores, mx, exp_chunk, since=-1, wide=0):
                for h in range(2):
                    if since == 2 and h == 1:
                        cut(c + 1, 2, exp_chunk)
                    if not mx:
                        continue
                    mc, mg, mpar = mx
                    n = 2 * mg + h
                    j2, qt, kc = n // (GT * KC), n // KC % GT, n % KC
                    dve.wait_ge(m_ready, MAXOPS * mc + n + 1)
                    if n == 0 and exp_chunk:
                        dve.wait_ge(negmax_ready, mc - 1)
                    dve.tensor_reduce(pmax[mpar][:, :, j2, qt, kc], psM[:, h, :, :], AX.X, ALU.max).then_inc(m_done, 1)
                if since == 0:
                    dve.wait_ge(m_done, MAXOPS * (c + 2) + 2)
                    if exp_chunk:
                        dve.wait_ge(negmax_turned, c + 1)
                    dve.tensor_reduce(negmax[:, 0:4 * GT].rearrange("p (a b) -> p a b", b=GT),
                                      pmax[1 - par][:].rearrange("p i j t k -> p (i j) t k"), AX.X, ALU.max,
                                      negate=True).then_inc(negmax_ready, 1)
                if since == 1:
                    cut(c + 1, 0, exp_chunk)
                    cut(c + 1, 1, exp_chunk)
                elif since == 2:
                    cut(c + 1, 3, exp_chunk)
                if exp_chunk and kt == 0:
                    turned = psT[:].rearrange("p j (g w) -> p (j g) w", g=HG)
                    dve.wait_ge(ctx_turned, c + 2)
                    dve.reciprocal(rden[:].unsqueeze(2), turned[:, :, DH:VW]).then_inc(rden_ready, 1)
                    dve.wait_ge(rden_ready, c + 1)
                    dst = ctx_tok[:, bass.ds(c * GT, GT), :]
                    dve.tensor_tensor(dst.rearrange("p j (g d) -> p j g d", g=HG),
                                      psT[:].rearrange("p j (g w) -> p j g w", g=HG)[:, :, :, 0:DH],
                                      rden[:].rearrange("p (j g) -> p j g", g=HG).unsqueeze(3).broadcast_to([P, GT, HG, DH]),
                                      ALU.mult).then_inc(ctx_done, 1)

            def last_experts(part, g, par):
                experts(part, g, par)
                if part > FC:
                    dve.wait_ge(y_done, NG + 1)
                    dve.memset(psO[:], 0.0).then_inc(acc_saved, 1)

            def output(g, turn_next, add_before=True):
                if g == NG - 1 and turn_next:
                    dve.wait_ge(ctx_done, last_chunk(g) + 2)
                    dve.wait_ge(turned, g - 1)
                    dve.tensor_copy(ctx_g[g % 2][:].rearrange("p j (u e) -> p j u e", u=NHG), heads_of(g)).then_inc(gathered, 1)
                if turn_next:
                    dve.wait_ge(turned, g + 1)
                    if g >= 2:
                        dve.wait_ge(projected, g - 1)
                    dve.tensor_copy(ctxT[g % 2][:], psC).then_inc(copied, 1)
                if g >= 1 and add_before:
                    dve.wait_ge(projected, g)
                    mine = y_tok[:, (g - 1) * GT:g * GT, :]
                    dve.tensor_tensor(mine, psW, mine, ALU.add).then_inc(added, 1)

            all_chunks(dve, step, last_experts, output, lag=1)

        @block.scalar
        def _(act):
            def project(part, g, par, first, last):
                if part == 0:
                    act.wait_ge(xnT_turned, g + 1)
                    act.copy(xnT[par][:], psA).then_inc(xnT_ready, 1)
                elif part == 1:
                    if not first:
                        act.wait_ge(v_kept, 4 * g)
                        act.wait_ge(am_ready, g)
                    for j in range(GT):
                        act.wait_ge(vga_ps, 4 * g + j + 1)
                        act.copy(raw[:, j, :], psV[:, j % 2, 0:W3]).then_inc(raw_copied, 1)
                elif part == 2:
                    act.wait_ge(lg_ready, g + 1)
                    act.activation(ex[:], lg[:], ACT.Exp).then_inc(ex_ready, 1)
                    act.wait_ge(qk_ps, g + 1)
                    if first:
                        act.wait_ge(w_loaded, 16 * NW)
                        act.wait_ge(scaled, 2)
                        act.wait_ge(w_rest, 16 * 5)
                    else:
                        act.wait_ge(parts_ready, g)
                    act.activation(qk32[:, 0, :], psQK[:, 0, :], ACT.Identity, bias=qbs[:, 0:1], scale=SCALE)
                    act.activation(qk32[:, 1, :], psQK[:, 1, :], ACT.Identity, bias=kb[:, 0:1]).then_inc(qk32_ready, 1)
                elif part == 3:
                    act.wait_ge(qk32_ready, g + 1)
                    if not first:
                        act.wait_ge(parts_stored, 32 * g)
                    act.copy(parts[:, :, 0, :], qk32[:]).then_inc(hi_ready, 1)

            def experts(part, g, par):
                for f, s, n in hidden(part):
                    act.wait_ge(h_added, 4 * g + f + 1)
                    act.wait_ge(z_ready, 8 * g + n)
                    act.activation(hs[f % 2][s], psZ[:, f % 2, :], ACT.Relu, bias=bi[:, f:f + 1]).then_inc(z_read, 1)

            def masked(g, par, first, last):
                for s in range(2):
                    act.wait_ge(amT_turned, g + 1)
                    ins = act.copy(amT[par][s][:], psV[:, s, :])
                ins.then_inc(amT_ready, 1)
                act.wait_ge(rest_ready, g + 1)
                act.copy(parts[:, :, 1, :], rest[:]).then_inc(mid_ready, 1)

            act.sem_inc(z_read, 2)
            run(act, schedule(project, experts, masked))

            def step(c, par, cc, kt, cpar, with_scores, mx, exp_chunk, since=-1, wide=0):
                for j2 in range(2):
                    if with_scores:
                        if j2 == 0:
                            act.wait_ge(pv_done, KT * cc + kt + 1)
                        for jj in range(2):
                            n = TILES * cc + HG * kt + 2 * j2 + jj
                            act.wait_ge(scores_ready, n + 1)
                            act.activation(probs[:, kt % 2, 2 * j2 + jj, :], score_bank(j2, jj, wide), ACT.Exp).then_inc(exp_done, 1)
                    if j2 == 0 and kt == 0 and exp_chunk:
                        act.wait_ge(pv_done, KT * (c + 1) + 2)
                        act.wait_ge(ctx_turned, c + 1)
                        act.copy(acc_sb[:], psO[:]).then_inc(acc_saved, 1)

            act.sem_inc(exp_done, 2)
            all_chunks(act, step, experts, lambda *_: None)

        @block.tensor
        def _(pe):
            def turn_x(g, first):
                pe.wait_ge(xn_ready, g + 1)
                if first:
                    pe.wait_ge(consts, NCONST)
                else:
                    pe.wait_ge(xnT_ready, g)
                for j in range(GT):
                    mm = pe.transpose(psA[:, j * P:(j + 1) * P], xn[:, j, :], ident[:])
                mm.then_inc(xnT_turned, 1)

            def project(part, g, par, first, last):
                if part == 0:
                    turn_x(g, first)
                elif part == 1:
                    pe.wait_ge(xnT_ready, g + 1)
                    if first:
                        pe.wait_ge(w_loaded, 16 * NW)
                    for j in range(GT):
                        if j < 2:
                            if not first:
                                pe.wait_ge(amT_ready, g)
                        else:
                            pe.wait_ge(raw_copied, 4 * g + j - 1)
                        pe.matmul(psV[:, j % 2, 0:W3], xnT[par][:, j * P:(j + 1) * P], w3[:],
                                  start=True, stop=True).then_inc(vga_ps, 1)
                elif part == 2:
                    if not first:
                        pe.wait_ge(hi_ready, g)
                    pe.matmul(psQK[:, 0, :], wq[:], xnT[par][:], start=True, stop=True)
                    pe.matmul(psQK[:, 1, :], wk[:], xnT[par][:], start=True, stop=True).then_inc(qk_ps, 1)

            def experts(part, g, par):
                if part == 0:
                    pe.wait_ge(amT_ready, g + 1)
                for f, s, n in hidden(part):
                    before = ORDER.index((f, 0)) + 1 if s else (ORDER.index((f - 2, 1)) + 1 if f >= 2 else f - 1)
                    pe.wait_ge(z_read, 8 * g + before + 2)
                    z, fs = psZ[:, f % 2, :], slice(f * P, (f + 1) * P)
                    if s == 0:
                        pe.matmul(z, wi[:, fs], xnT[par][:], start=True, stop=False, skip_group_check=True)
                    pe.matmul(z, lora_b[:, fs], amT[par][s][:], start=False, stop=(s == 1),
                              skip_group_check=True).then_inc(z_ready, 1)
                if part < FC:
                    return
                for f in range(2) if part == FC else range(2, FC):
                    pe.wait_ge(h_added, 4 * g + f + 1 + 2)
                    for j in range(GT):
                        mm = pe.matmul(psY[:, j, :], hT[:, f, j * P:(j + 1) * P], wo[:, f, :],
                                       start=(f == 0 and j == 0), stop=(f == FC - 1), skip_group_check=True)
                if part > FC:
                    mm.then_inc(y_ps, 1)

            def masked(g, par, first, last):
                if first:
                    pe.wait_ge(w_rest, 16 * 5)
                pe.wait_ge(am_ready, g + 1)
                pe.wait_ge(raw_copied, 4 * g + 4)
                for s in range(2):
                    for j in range(GT):
                        mm = pe.transpose(psV[:, s, j * P:(j + 1) * P], am[s][:, j, :], ident[:])
                mm.then_inc(amT_turned, 1)

            run(pe, schedule(project, experts, masked))

            def max_scores(mc, mg, mpar, h, jj):
                op = MAXOPS * mc + 2 * mg + h
                n = 2 * mg + h
                j2, qt, kc = n // (GT * KC), n // KC % GT, n % KC
                if n == 0 and jj == 0:
                    pe.wait_ge(m_loaded[mpar], (mc // 2 + 1) * (16 * NLOAD))
                if jj == 0:
                    pe.wait_ge(m_done, op + 1)
                mm = pe.matmul(psM[:, h, jj, :], qM[mpar][:, jj, j2, qt * P:(qt + 1) * P],
                               kM[mpar][:, j2, kc * G:(kc + 1) * G], start=True, stop=True)
                if jj == 1:
                    mm.then_inc(m_ready, 1)

            def scores(cc, kt, cpar, j2, jj, wide):
                if kt == 0 and j2 == 0 and jj == 0:
                    pe.wait_ge(e_loaded, (cc + 1) * (16 * NCOPY))
                    pe.wait_ge(rows_loaded, (cc + 1) * (16 * NROWS))
                tile = TILES * cc + HG * kt + 2 * j2 + jj
                if wide == 1 and j2 == 1:
                    pe.wait_ge(m_done, MAXOPS * NCH + 2)
                elif wide > 1:
                    pe.wait_ge(exp_done, tile - 1)
                else:
                    pe.wait_ge(exp_done, tile + 1)
                pe.matmul(score_bank(j2, jj, wide), kE[cpar][:, j2, kt * P:(kt + 1) * P], qE[cpar][:, jj, j2, :],
                          start=True, stop=True).then_inc(scores_ready, 1)

            def products(c, kt, par):
                if kt == 0:
                    pe.wait_ge(acc_saved, c + 1)
                pe.wait_ge(exp_done, TILES * c + HG * (kt + 1) + 2)
                for g in range(HG):
                    mm = pe.matmul(psO[32 * g:32 * g + VW, :], v[par][:, (HG * kt + g) * VW:(HG * kt + g + 1) * VW],
                                   probs[:, kt % 2, g, :], start=(kt == 0), stop=(kt == KT - 1))
                mm.then_inc(pv_done, 1)

            def step(c, par, cc, kt, cpar, with_scores, mx, exp_chunk, since=-1, wide=0):
                for j2 in range(2):
                    for jj in range(2):
                        if with_scores:
                            scores(cc, kt, cpar, j2, jj, wide)
                    if exp_chunk and j2 == (1 if wide > 0 else 0):
                        products(c, (kt - 1) % KT, par)
                if mx:
                    for h in range(2):
                        for jj in range(2):
                            max_scores(*mx, h, jj)
                if since == 1:
                    pe.wait_ge(negmax_ready, c + 2)
                    if exp_chunk:
                        pe.wait_ge(ctx_done, c + 1)
                    pe.transpose(psT[:, 0, :], negmax[:], ident[:]).then_inc(negmax_turned, 1)
                if exp_chunk and kt == 0:
                    pe.wait_ge(acc_saved, c + 2)
                    if isinstance(c, int) and c == NCH - 1:
                        pe.wait_ge(ctx_done, c + 1)
                    else:
                        pe.wait_ge(rows_ready, c + 2)
                    for j in range(GT):
                        tr = pe.transpose(psT[:, j, :], acc_sb[:, j * P:(j + 1) * P], ident[:])
                    tr.then_inc(ctx_turned, 1)

            def output(g, turn_next, project_before=True):
                if turn_next:
                    pe.wait_ge(gathered, g + 1)
                    if g == 0:
                        pe.wait_ge(m_done, MAXOPS * NCH + 2)
                    if g >= 1:
                        pe.wait_ge(copied, g)
                    for j in range(GT):
                        tr = pe.transpose(psC[:, j * P:(j + 1) * P], ctx_g[g % 2][:, j, :], ident[:])
                    tr.then_inc(turned, 1)
                if g >= 1 and project_before:
                    pe.wait_ge(copied, g)
                    if g >= 2:
                        pe.wait_ge(added, g - 1)
                    for j in range(GT):
                        mm = pe.matmul(psW[:, j, :], ctxT[(g - 1) % 2][:, j * P:(j + 1) * P], out_w[:],
                                       start=True, stop=True)
                    mm.then_inc(projected, 1)

            pe.wait_ge(amT_ready, NG)
            pe.sem_inc(pv_done, 2)
            pe.sem_inc(ctx_turned, 1)
            all_chunks(pe, step, experts, output)


def kernel(L0_attn_query, L0_attn_mask, L0_attn_q_w, L0_attn_q_b, L0_attn_k_w, L0_attn_k_b, L0_attn_v_w, L0_attn_v_b,
           L0_attn_out_w, L0_attn_out_b, L0_ffn_wi, L0_ffn_bi, L0_ffn_wo, L0_ffn_bo, L0_ffn_lora_A, L0_ffn_lora_B,
           L0_ffn_gate_w, L0_ffn_gate_b):
    import numpy as np
    import concourse.bacc as bacc
    from concourse.bass_utils import run_bass_kernel_spmd

    c = np.ascontiguousarray
    lay = {
        "x": c(np.asarray(L0_attn_query)),
        "q_wT": c(np.asarray(L0_attn_q_w).T), "k_wT": c(np.asarray(L0_attn_k_w).T),
        "v_wT": c(np.asarray(L0_attn_v_w).T), "out_wT": c(np.asarray(L0_attn_out_w).T),
        "q_b": c(L0_attn_q_b), "k_b": c(L0_attn_k_b), "v_b": c(L0_attn_v_b), "out_b": c(L0_attn_out_b),
        "gate_wT": c(np.asarray(L0_ffn_gate_w).T), "gate_b": c(L0_ffn_gate_b),
        "wiT": c(np.asarray(L0_ffn_wi).T), "bi": c(np.asarray(L0_ffn_bi).reshape(FC, P).T), "woT": c(np.asarray(L0_ffn_wo).T), "bo": c(L0_ffn_bo),
        "lora_AT": c(np.asarray(L0_ffn_lora_A).reshape(E * R, D).T),
        "lora_BT": c(np.asarray(L0_ffn_lora_B).transpose(0, 2, 1).reshape(E * R, F)),
    }
    nc = bacc.Bacc("TRN2", target_bir_lowering=False, num_devices=1)
    io = {n: nc.dram_tensor(f"in_{n}", a.shape, F32, kind="ExternalInput").ap() for n, a in lay.items()}
    out = nc.dram_tensor("out", (B, S, D), F32, kind="ExternalOutput").ap()
    io["x"] = io["x"].rearrange("b (n p) d -> p (b n) d", p=P)
    io["out"] = out.rearrange("b (n p) d -> p (b n) d", p=P)
    io["woT"] = io["woT"].rearrange("(f p) d -> p f d", p=P)
    io["q_b"] = io["q_b"].unsqueeze(1)
    io["k_b"] = io["k_b"].unsqueeze(1)
    io["scratch"] = nc.dram_tensor("qk_parts", (2, NPART, B, D, S), BF16, kind="Internal").ap()
    program(nc, io)
    r = run_bass_kernel_spmd(nc, [{f"in_{n}": a for n, a in lay.items()}], core_ids=[0])
    return r.results[0]["out"]
```
